# Optimizing a Trainium2 kernel written in Bass

```python
import numpy as np
import jax
import jax.numpy as jnp

def _softmax(x, axis=-1):
    return jax.nn.softmax(x, axis=axis)
def _gelu(x):
    return jax.nn.gelu(x, approximate=True)
def _silu(x):
    return jax.nn.silu(x)
def _sigmoid(x):
    return jax.nn.sigmoid(x)
def _layernorm(x, axis=-1, eps=1e-5):
    m = jnp.mean(x, axis=axis, keepdims=True)
    v = jnp.var(x, axis=axis, keepdims=True)
    return (x - m) / jnp.sqrt(v + eps)
def _scatter_add(tgt, idx, src, axis=0):
    return tgt.at[idx].add(src)
def _segment_sum(src, seg, n):
    return jax.ops.segment_sum(src, seg, n)

kernel_name = 'mk_adj_seq_d1_adj_512_ac7c18'

def setup_inputs(seed: int = 0):
    np.random.seed(seed)
    _w = jnp.asarray
    def _rec_inputs():
        import jax
        import jax.numpy as jnp
        _gk = jax.random.key(seed)
        x = 7.22e-05 + 1 * jax.random.normal(jax.random.fold_in(_gk, 1), (32, 512, 512), jnp.float32)
        _w = (1.0 + jnp.arange(512, dtype=jnp.float32)) ** -0.5
        _w = _w / _w.mean()
        _pij = jnp.clip(0.0078125 * _w[:, None] * _w[None, :], 0.0, 1.0)
        _a = jax.random.uniform(jax.random.fold_in(_gk, 2), (32, 512, 512)) < _pij
        adj = _a.astype(jnp.int32)
        return x, adj
    x, adj = _rec_inputs()
    def _L0_gnn_setup():
        import jax, jax.numpy as jnp
        import numpy as np
        import math
        D = 512
        B, L = (8, 2048)
        EPS = 1e-05

        def layer_norm(y, gamma, beta):
            mu = jnp.mean(y, axis=-1, keepdims=True)
            var = jnp.mean(jnp.square(y - mu), axis=-1, keepdims=True)
            return (y - mu) * jax.lax.rsqrt(var + EPS) * gamma + beta
        key = jax.random.key(seed)
        ks = jax.random.split(key, 8)
        s = 1.0 / math.sqrt(D)
        x = jax.random.normal(ks[0], (B, L, D), dtype=jnp.float32)
        adj = jax.random.randint(ks[1], (B, L, L), 0, 2, dtype=jnp.int32)
        Wq = jax.random.normal(ks[2], (D, D), dtype=jnp.float32) * s
        Wk = jax.random.normal(ks[3], (D, D), dtype=jnp.float32) * s
        Wv = jax.random.normal(ks[4], (D, D), dtype=jnp.float32) * s
        Wo = jax.random.normal(ks[5], (D, D), dtype=jnp.float32) * s
        bo = jnp.zeros((D,), dtype=jnp.float32)
        gamma = jnp.ones((D,), dtype=jnp.float32)
        beta = jnp.zeros((D,), dtype=jnp.float32)
        return {'x': x, 'adj': adj, 'Wq': Wq, 'Wk': Wk, 'Wv': Wv, 'Wo': Wo, 'bo': bo, 'gamma': gamma, 'beta': beta}
    _L0_gnn_all = _L0_gnn_setup()
    _L0_gnn_in = {k: v for k, v in _L0_gnn_all.items() if k in ('Wq', 'Wk', 'Wv', 'Wo', 'bo', 'gamma', 'beta', )}
    del _L0_gnn_all

    return {
        "x": x,
        "adj": adj,
        "L0_gnn_Wq": _L0_gnn_in["Wq"],
        "L0_gnn_Wk": _L0_gnn_in["Wk"],
        "L0_gnn_Wv": _L0_gnn_in["Wv"],
        "L0_gnn_Wo": _L0_gnn_in["Wo"],
        "L0_gnn_bo": _L0_gnn_in["bo"],
        "L0_gnn_gamma": _L0_gnn_in["gamma"],
        "L0_gnn_beta": _L0_gnn_in["beta"],
    }

def reference(x, adj, L0_gnn_Wq, L0_gnn_Wk, L0_gnn_Wv, L0_gnn_Wo, L0_gnn_bo, L0_gnn_gamma, L0_gnn_beta):
    import jax
    import jax.numpy as jnp
    def _L0_gnn_ref(x, adj, Wq, Wk, Wv, Wo, bo, gamma, beta):
        import jax, jax.numpy as jnp
        import numpy as np
        import math
        D = 512
        B, L = (8, 2048)
        EPS = 1e-05

        def layer_norm(y, gamma, beta):
            mu = jnp.mean(y, axis=-1, keepdims=True)
            var = jnp.mean(jnp.square(y - mu), axis=-1, keepdims=True)
            return (y - mu) * jax.lax.rsqrt(var + EPS) * gamma + beta
        d_out = Wq.shape[1]
        scale = 1.0 / math.sqrt(d_out)
        Q = x @ Wq
        K = x @ Wk
        V = x @ Wv
        sc = jnp.einsum('bld,bmd->blm', Q, K) * scale
        mask = adj == 0
        sc = jnp.where(mask, -jnp.inf, sc)
        all_inf = jnp.all(mask, axis=-1, keepdims=True)
        sc = jnp.where(all_inf, 0.0, sc)
        w = jax.nn.softmax(sc, axis=-1)
        out = jnp.einsum('blm,bmd->bld', w, V)
        y = x + out @ Wo + bo
        return layer_norm(y, gamma, beta)

    x = _L0_gnn_ref(x, adj, L0_gnn_Wq, L0_gnn_Wk, L0_gnn_Wv, L0_gnn_Wo, L0_gnn_bo, L0_gnn_gamma, L0_gnn_beta)
    return x


_drawn_inputs = setup_inputs


def setup_inputs(seed=0):
    import zlib

    import numpy as np

    out = dict(_drawn_inputs(seed))
    spreads = {'L0_gnn_bo': (0.0, 0.1), 'L0_gnn_gamma': (1.0, 0.2), 'L0_gnn_beta': (0.0, 0.1)}
    factors = {}
    for name, (base, spread) in spreads.items():
        noise = np.random.default_rng([zlib.crc32(name.encode()), seed]).standard_normal(out[name].shape)
        drawn = base * np.exp(spread * noise) if base else spread * noise
        out[name] = jnp.asarray(drawn.astype(out[name].dtype))
    for name, factor in factors.items():
        out[name] = (out[name] * factor).astype(out[name].dtype)
    return out
```

```python
from contextlib import ExitStack

import concourse.bass as bass
from concourse import mybir

F32 = mybir.dt.float32
F32R = mybir.dt.float32r
I32 = mybir.dt.int32
ALU = mybir.AluOpType
ACT = mybir.ActivationFunctionType

P = 128
EPS = 1e-5
MASKED = -(2.0 ** 126)


def graph_attention(nc, xT, x, adj, wqT, wkT, wvT, wo, bo, gamma, beta, out):
    B, L, D = x.shape
    C = D // P
    R = L // P
    assert L == D and C == R and B % 2 == 0
    SCALE = float(D) ** -0.5
    STEPS = R

    x_rows = x.rearrange("b (i p) d -> b p i d", p=P)
    adj_rows = adj.rearrange("b (i p) m -> b p i m", p=P)
    out_rows = out.rearrange("b (i p) d -> b p i d", p=P)

    with ExitStack() as ctx:
        def sb(name, shape, dt=F32):
            return ctx.enter_context(nc.sbuf_tensor(name, shape, dt))

        def sem(name):
            return ctx.enter_context(nc.semaphore(name))

        def split_pair(name):
            return sb(name + "_hi", [P, C, D], F32R), sb(name + "_lo", [P, C, D], F32R)

        m_qk = split_pair("m_qk")
        m_vo = split_pair("m_vo")
        x_t = [split_pair(f"x_t{k}") for k in range(2)]
        q_t = split_pair("q_t")
        v = [split_pair(f"v{k}") for k in range(2)]
        p_t = split_pair("p_t")
        x_t_raw = sb("x_t_raw", [P, C, L])
        adj_raw = sb("adj_raw", [P, R, L], I32)
        mask_add = sb("mask_add", [P, R, L])
        probs = sb("probs", [P, R, L])
        resid = [sb(f"resid{k}", [P, R, D]) for k in range(2)]
        y = [sb(f"y{k}", [P, R, D]) for k in range(2)]
        gamma_bc = sb("gamma_bc", [P, D])
        beta_bc = sb("beta_bc", [P, D])
        bo_bc = sb("bo_bc", [P, D])
        ident = sb("ident", [P, P])
        neg_max = sb("neg_max", [P, 2, R])
        row_sum = sb("row_sum", [P, 2, R])
        row_inv = sb("row_inv", [P, 2, R])
        stats = sb("stats", [P, 2, R, 6])
        mean_var = sb("mean_var", [P, 2, R, 2])
        var_eps = sb("var_eps", [P, 2, R])
        rstd = sb("rstd", [P, 2, R])
        neg_mean_rstd = sb("neg_mean_rstd", [P, 2, R])
        neg_mean = sb("neg_mean", [P, 2, R])
        minus_half = sb("minus_half", [P, R])
        minus_one = sb("minus_one", [P, R])
        eps = sb("eps", [P, R])
        wait_slot = sb("wait_slot", [P, 2, R, 2])
        banks = [ctx.enter_context(nc.psum_tensor(f"bank{k}", [P, 512], F32)) for k in range(8)]

        w_loaded = [sem(f"w_loaded{k}") for k in range(4)]
        ln_loaded = sem("ln_loaded")
        xt_loaded = sem("xt_loaded")
        adj_loaded = sem("adj_loaded")
        x_loaded = sem("x_loaded")
        w_hi = sem("w_hi")
        w_lo = sem("w_lo")
        m_ps = sem("m_ps")
        m_hi = sem("m_hi")
        m_lo = sem("m_lo")
        xt_hi = sem("xt_hi")
        xt_lo = sem("xt_lo")
        q_ps = sem("q_ps")
        q_hi = sem("q_hi")
        q_lo = sem("q_lo")
        v_ps = sem("v_ps")
        v_hi = sem("v_hi")
        v_lo = sem("v_lo")
        s_ps = sem("s_ps")
        mask_ready = sem("mask_ready")
        masked = sem("masked")
        exp_done = sem("exp_done")
        pt_ps = sem("pt_ps")
        pt_hi = sem("pt_hi")
        pt_lo = sem("pt_lo")
        o_ps = sem("o_ps")
        inv_ready = sem("inv_ready")
        resid_ready = sem("resid_ready")
        y_ready = sem("y_ready")
        stats_ready = sem("stats_ready")
        moments_ready = sem("moments_ready")
        rstd_step = sem("rstd_step")
        z_ready = sem("z_ready")
        scaled = sem("scaled")
        out_ready = sem("out_ready")
        stored = sem("stored")
        ident_zero = sem("ident_zero")
        ident_ready = sem("ident_ready")
        const_ready = sem("const_ready")

        w_raw = [resid[0], resid[1], y[0], y[1]]
        w_src = [wqT, wkT, wvT, wo]
        w_part = [v[0], v[1], p_t, q_t]

        def half_of(group):
            return banks[4 * (group % 2):4 * (group % 2) + 4]


        block = ctx.enter_context(nc.Block())

        @block.sync
        def _(sp):
            def load_xt(b):
                sp.dma_start(x_t_raw[:], xT[b]).then_inc(xt_loaded, 16)

            def load_adj(b):
                sp.dma_start(adj_raw[:], adj_rows[b]).then_inc(adj_loaded, 16)

            def load_x(b, par):
                sp.dma_start(resid[par][:], x_rows[b]).then_inc(x_loaded, 16)

            def store(b, par, first=False):
                if not first:
                    sp.wait_ge(stored, 16 * b)
                sp.wait_ge(out_ready, STEPS * b + STEPS)
                sp.dma_start(out_rows[b], y[par][:]).then_inc(stored, 16)

            def graph(b, par, ahead=2, behind=True, second=False):
                if ahead >= 1:
                    sp.wait_ge(mask_ready, b + 1)
                    load_adj(b + 1)
                    sp.wait_ge(resid_ready, STEPS * b + STEPS)
                    if behind:
                        sp.wait_ge(y_ready, STEPS * b)
                    load_x(b + 1, 1 - par)
                if ahead >= 2:
                    sp.wait_ge(xt_lo, STEPS * b + 2 * STEPS)
                    load_xt(b + 2)
                if behind:
                    store(b - 1, 1 - par, first=second)

            for k in range(4):
                sp.dma_start(w_raw[k][:], w_src[k].rearrange("(c p) n -> p c n", p=P)).then_inc(w_loaded[k], 16)
                if k == 1:
                    load_xt(0)
            for row, tile in ((gamma, gamma_bc), (beta, beta_bc), (bo, bo_bc)):
                sp.dma_start(tile[:], row.rearrange("(a d) -> a d", a=1).broadcast_to([P, D])).then_inc(ln_loaded, 16)
            load_adj(0)
            sp.wait_ge(xt_lo, STEPS)
            load_xt(1)
            sp.wait_ge(w_lo, 4)
            load_x(0, 0)
            graph(0, 0, behind=False)
            graph(1, 1, second=True)
            with sp.Fori(2, B - 4, 2) as b:
                graph(b, 0)
                graph(b + 1, 1)
            graph(B - 4, 0)
            graph(B - 3, 1)
            graph(B - 2, 0, ahead=1)
            graph(B - 1, 1, ahead=0)
            store(B - 1, 1)
            sp.wait_ge(stored, 16 * B)

        @block.tensor
        def _(pe):
            def product(bank, a, a_cols, b, signal):
                (a_hi, a_lo), (b_hi, b_lo) = a, b
                for c in range(C):
                    pe.matmul(bank[:], a_hi[:, c, a_cols], b_hi[:, c, :], start=(c == 0), stop=False)
                    pe.matmul(bank[:], a_hi[:, c, a_cols], b_lo[:, c, :], start=False, stop=False)
                    last = pe.matmul(bank[:], a_lo[:, c, a_cols], b_hi[:, c, :], start=False, stop=(c == C - 1))
                last.then_inc(signal, 1)

            def cols(k):
                return slice(P * k, P * k + P)

            def scores(b, par, first):
                pe.wait_ge(q_lo, STEPS * b + STEPS)
                if not first:
                    pe.wait_ge(v_lo, STEPS * b + STEPS)
                for i in range(R):
                    product(half_of(par)[i], q_t, cols(i), x_t[par], s_ps)

            def queries(b, par, first=False):
                pe.wait_ge(xt_lo, STEPS * b + STEPS)
                if first:
                    pe.wait_ge(v_lo, STEPS)
                else:
                    pe.wait_ge(y_ready, STEPS * b - STEPS)
                for e in range(C):
                    product(half_of(par)[e], m_qk, cols(e), x_t[par], q_ps)

            def transposes(b, par):
                for i in range(R):
                    pe.wait_ge(exp_done, STEPS * b + i + 1)
                    for j in range(R):
                        last = pe.transpose(half_of(par)[i][:, cols(j)], probs[:, i, cols(j)], ident[:])
                    last.then_inc(pt_ps, 1)

            def values(b, par, half):
                for m in range(R):
                    if half == par:
                        pe.wait_ge(q_lo, STEPS * b + m + 1)
                    product(half_of(half)[m], x_t[par], cols(m), m_vo, v_ps)

            def attend(b, par):
                p_hi, p_lo = p_t
                v_hi_part, v_lo_part = v[par]
                for i in range(R):
                    pe.wait_ge(pt_lo, STEPS * b + i + 1)
                    bank = half_of(par)[i]
                    for j in range(R):
                        at = slice(P * j, P * j + P)
                        pe.matmul(bank[:], p_hi[:, i, at], v_hi_part[:, j, :], start=(j == 0), stop=False)
                        pe.matmul(bank[:], p_hi[:, i, at], v_lo_part[:, j, :], start=False, stop=False)
                        last = pe.matmul(bank[:], p_lo[:, i, at], v_hi_part[:, j, :], start=False, stop=(j == R - 1))
                    last.then_inc(o_ps, 1)

            pe.wait_ge(w_lo, 2)
            for d in range(C):
                product(half_of(0)[d], w_part[0], cols(d), w_part[1], m_ps)
            pe.wait_ge(w_lo, 4)
            for d in range(C):
                product(half_of(1)[d], w_part[2], cols(d), w_part[3], m_ps)
            pe.wait_ge(m_lo, C)
            pe.wait_ge(xt_lo, STEPS)
            for e in range(C):
                product(half_of(0)[e], m_qk, cols(e), x_t[0], q_ps)
            pe.wait_ge(m_lo, 2 * C)
            values(0, 0, 1)

            def graph(b, par, first=False, last=False):
                scores(b, par, first)
                if not last:
                    queries(b + 1, 1 - par, first=first)
                if first:
                    pe.wait_ge(ident_ready, 1)
                transposes(b, par)
                if not last:
                    values(b + 1, 1 - par, 1 - par)
                attend(b, par)

            graph(0, 0, first=True)
            with pe.Fori(1, B - 1, 2) as b:
                graph(b, 1)
                graph(b + 1, 0)
            graph(B - 1, 1, last=True)

        @block.scalar
        def _(act):
            def high(dst, src, signal):
                act.activation(dst, src, ACT.Copy).then_inc(signal, 1)

            def split_xt(b, par):
                act.wait_ge(xt_loaded, 16 * b + 16)
                for c in range(C):
                    high(x_t[par][0][:, c, :], x_t_raw[:, c, :], xt_hi)

            def exponentials(b, par, first=False):
                if not first:
                    act.wait_ge(pt_ps, STEPS * b)
                for i in range(R):
                    act.wait_ge(masked, STEPS * b + i + 1)
                    act.activation(probs[:, i, :], half_of(par)[i][:], ACT.Exp, bias=neg_max[:, par, i:i + 1],
                                   scale=-1.0, accum_out=row_sum[:, par, i:i + 1]).then_inc(exp_done, 1)

            def normalise(b, par):
                act.wait_ge(rstd_step, 4 * b + 4)
                for i in range(R):
                    act.activation(y[par][:, i, :], y[par][:, i, :], ACT.Identity,
                                   bias=neg_mean_rstd[:, par, i:i + 1], scale=rstd[:, par, i:i + 1]).then_inc(z_ready, 1)

            def high_q(b, par):
                for e in range(C):
                    act.wait_ge(q_ps, STEPS * b + e + 1)
                    high(q_t[0][:, e, :], half_of(par)[e][:], q_hi)

            def high_v(b, par, half):
                for m in range(R):
                    act.wait_ge(v_ps, STEPS * b + m + 1)
                    high(v[par][0][:, m, :], half_of(half)[m][:], v_hi)

            def high_pt(b, par):
                for i in range(R):
                    act.wait_ge(pt_ps, STEPS * b + i + 1)
                    high(p_t[0][:, i, :], half_of(par)[i][:], pt_hi)

            for k in range(2):
                act.wait_ge(w_loaded[k], 16)
                high(w_part[k][0][:], w_raw[k][:], w_hi)
            split_xt(0, 0)
            for k in range(2, 4):
                act.wait_ge(w_loaded[k], 16)
                high(w_part[k][0][:], w_raw[k][:], w_hi)
            for k, m in enumerate((m_qk, m_vo)):
                for d in range(C):
                    act.wait_ge(m_ps, C * k + d + 1)
                    high(m[0][:, d, :], half_of(k)[d][:], m_hi)
            high_q(0, 0)
            high_v(0, 0, 1)
            split_xt(1, 1)

            def graph(b, par, ahead=2, behind=True):
                exponentials(b, par, first=not behind)
                if behind:
                    normalise(b - 1, 1 - par)
                if ahead >= 1:
                    high_q(b + 1, 1 - par)
                if ahead >= 2:
                    act.wait_ge(s_ps, STEPS * b + STEPS)
                    split_xt(b + 2, par)
                high_pt(b, par)
                if ahead >= 1:
                    high_v(b + 1, 1 - par, 1 - par)

            graph(0, 0, behind=False)
            with act.Fori(1, B - 3, 2) as b:
                graph(b, 1)
                graph(b + 1, 0)
            graph(B - 3, 1)
            graph(B - 2, 0, ahead=1)
            graph(B - 1, 1, ahead=0)
            normalise(B - 1, 1)

        @block.vector
        def _(dve):
            def low(dst, src, high_part, signal):
                dve.tensor_tensor(dst, src, high_part.bitcast(F32), ALU.subtract).then_inc(signal, 1)

            def split_xt(b, par):
                for c in range(C):
                    dve.wait_ge(xt_hi, STEPS * b + c + 1)
                    low(x_t[par][1][:, c, :], x_t_raw[:, c, :], x_t[par][0][:, c, :], xt_lo)

            def additive_mask(b):
                dve.wait_ge(adj_loaded, 16 * b + 16)
                dve.tensor_scalar(mask_add[:], adj_raw[:], 0.0, MASKED, ALU.is_equal, ALU.mult).then_inc(mask_ready, 1)

            def hold_wait(par, i, use):
                dve.memset(wait_slot[:, par, i, use:use + 1], 0.0)

            def mask_scores(b, par, i):
                if i == 0:
                    dve.wait_ge(mask_ready, b + 1)
                dve.wait_ge(s_ps, STEPS * b + i + 1)
                hold_wait(par, i, 0)
                bank = half_of(par)[i]
                dve.tensor_tensor_reduce(bank[:], bank[:], mask_add[:, i, :], -SCALE, 3.0e38, ALU.add, ALU.min,
                                         neg_max[:, par, i:i + 1]).then_inc(masked, 1)

            def moments(b, par, i):
                dve.wait_ge(y_ready, STEPS * b + i + 1)
                dve.bn_stats(stats[:, par, i, :], y[par][:, i, :]).then_inc(stats_ready, 1)
                dve.wait_ge(stats_ready, STEPS * b + i + 1)
                hold_wait(par, i, 1)
                dve.bn_aggr(mean_var[:, par, i, :], stats[:, par, i, :]).then_inc(moments_ready, 1)

            def low_q(b, par):
                for e in range(C):
                    dve.wait_ge(q_hi, STEPS * b + e + 1)
                    low(q_t[1][:, e, :], half_of(par)[e][:], q_t[0][:, e, :], q_lo)

            def low_v(b, par, half):
                for m in range(R):
                    dve.wait_ge(v_hi, STEPS * b + m + 1)
                    low(v[par][1][:, m, :], half_of(half)[m][:], v[par][0][:, m, :], v_lo)

            def low_pt(b, par):
                for i in range(R):
                    dve.wait_ge(pt_hi, STEPS * b + i + 1)
                    low(p_t[1][:, i, :], half_of(par)[i][:], p_t[0][:, i, :], pt_lo)

            def outputs(b, par, reuse):
                dve.wait_ge(exp_done, STEPS * b + STEPS)
                dve.reciprocal(row_inv[:, par, :], row_sum[:, par, :]).then_inc(inv_ready, 1)
                dve.wait_ge(inv_ready, b + 1)
                dve.wait_ge(resid_ready, STEPS * b + STEPS)
                if reuse:
                    dve.wait_ge(stored, 16 * b - 16)
                for i in range(R):
                    dve.wait_ge(o_ps, STEPS * b + i + 1)
                    dve.scalar_tensor_tensor(y[par][:, i, :], half_of(par)[i][:], row_inv[:, par, i:i + 1],
                                             resid[par][:, i, :], ALU.mult, ALU.add).then_inc(y_ready, 1)

            for k in range(2):
                dve.wait_ge(w_hi, k + 1)
                low(w_part[k][1][:], w_raw[k][:], w_part[k][0][:], w_lo)
            split_xt(0, 0)
            for k in range(2, 4):
                dve.wait_ge(w_hi, k + 1)
                low(w_part[k][1][:], w_raw[k][:], w_part[k][0][:], w_lo)
            for k, m in enumerate((m_qk, m_vo)):
                for d in range(C):
                    dve.wait_ge(m_hi, C * k + d + 1)
                    low(m[1][:, d, :], half_of(k)[d][:], m[0][:, d, :], m_lo)
            additive_mask(0)
            low_q(0, 0)
            low_v(0, 0, 1)
            split_xt(1, 1)

            def graph(b, par, ahead=2, behind=True, reuse=True):
                for i in range(R):
                    mask_scores(b, par, i)
                    if behind:
                        moments(b - 1, 1 - par, i)
                if ahead >= 1:
                    low_q(b + 1, 1 - par)
                    additive_mask(b + 1)
                if ahead >= 2:
                    split_xt(b + 2, par)
                low_pt(b, par)
                if ahead >= 1:
                    low_v(b + 1, 1 - par, 1 - par)
                outputs(b, par, reuse)

            graph(0, 0, behind=False, reuse=False)
            graph(1, 1, reuse=False)
            with dve.Fori(2, B - 2, 2) as b:
                graph(b, 0)
                graph(b + 1, 1)
            graph(B - 2, 0, ahead=1)
            graph(B - 1, 1, ahead=0)
            for i in range(R):
                moments(B - 1, 1, i)

        @block.gpsimd
        def _(pool):
            pool.memset(minus_half[:], -0.5).then_inc(const_ready, 1)
            pool.memset(minus_one[:], -1.0).then_inc(const_ready, 1)
            pool.memset(eps[:], EPS).then_inc(const_ready, 1)
            pool.memset(ident[:], 0.0).then_inc(ident_zero, 1)
            pool.wait_ge(ident_zero, 1)
            pool.affine_select(out=ident[:], in_=ident[:], compare_op=ALU.not_equal, fill=1.0, base=0,
                               pattern=[[-1, P]], channel_multiplier=1).then_inc(ident_ready, 1)
            pool.wait_ge(const_ready, 3)
            pool.wait_ge(ln_loaded, 48)

            def residual(b, par):
                pool.wait_ge(x_loaded, 16 * b + 16)
                for i in range(R):
                    pool.tensor_tensor(resid[par][:, i, :], resid[par][:, i, :], bo_bc[:], ALU.add).then_inc(resid_ready, 1)

            def deviation(b, par):
                pool.wait_ge(moments_ready, STEPS * b + STEPS)
                pool.tensor_tensor(var_eps[:, par, :], mean_var[:, par, :, 1], eps[:], ALU.add).then_inc(rstd_step, 1)
                pool.wait_ge(rstd_step, 4 * b + 1)
                pool.tensor_tensor(rstd[:, par, :], var_eps[:, par, :], minus_half[:], ALU.pow).then_inc(rstd_step, 1)
                pool.tensor_tensor(neg_mean[:, par, :], mean_var[:, par, :, 0], minus_one[:], ALU.mult).then_inc(rstd_step, 1)
                pool.wait_ge(rstd_step, 4 * b + 3)
                pool.tensor_tensor(neg_mean_rstd[:, par, :], neg_mean[:, par, :], rstd[:, par, :], ALU.mult).then_inc(rstd_step, 1)

            def affine(b, par):
                for i in range(R):
                    pool.wait_ge(z_ready, STEPS * b + i + 1)
                    pool.tensor_tensor(y[par][:, i, :], y[par][:, i, :], gamma_bc[:], ALU.mult).then_inc(scaled, 1)
                for i in range(R):
                    pool.wait_ge(scaled, STEPS * b + i + 1)
                    pool.tensor_tensor(y[par][:, i, :], y[par][:, i, :], beta_bc[:], ALU.add).then_inc(out_ready, 1)

            residual(0, 0)
            with pool.Fori(0, B - 2, 2) as b:
                residual(b + 1, 1)
                deviation(b, 0)
                affine(b, 0)
                residual(b + 2, 0)
                deviation(b + 1, 1)
                affine(b + 1, 1)
            residual(B - 1, 1)
            deviation(B - 2, 0)
            affine(B - 2, 0)
            deviation(B - 1, 1)
            affine(B - 1, 1)


def kernel(x, adj, L0_gnn_Wq, L0_gnn_Wk, L0_gnn_Wv, L0_gnn_Wo, L0_gnn_bo, L0_gnn_gamma, L0_gnn_beta):
    import numpy as np
    import concourse.bacc as bacc
    from concourse.bass_utils import run_bass_kernel_spmd

    x = np.asarray(x)
    B, L, D = x.shape
    arrays = {
        "xT": np.ascontiguousarray(x.transpose(0, 2, 1).reshape(B, D // P, P, L).transpose(0, 2, 1, 3)),
        "x": np.ascontiguousarray(x),
        "adj": np.ascontiguousarray(np.asarray(adj)),
        "wqT": np.ascontiguousarray(np.asarray(L0_gnn_Wq).T),
        "wkT": np.ascontiguousarray(np.asarray(L0_gnn_Wk).T),
        "wvT": np.ascontiguousarray(np.asarray(L0_gnn_Wv).T),
        "wo": np.ascontiguousarray(np.asarray(L0_gnn_Wo)),
        "bo": np.ascontiguousarray(np.asarray(L0_gnn_bo)),
        "gamma": np.ascontiguousarray(np.asarray(L0_gnn_gamma)),
        "beta": np.ascontiguousarray(np.asarray(L0_gnn_beta)),
    }
    nc = bacc.Bacc("TRN2", target_bir_lowering=False, num_devices=1)
    args = [nc.dram_tensor(f"in_{n}", a.shape, mybir.dt.from_np(a.dtype), kind="ExternalInput").ap() for n, a in arrays.items()]
    out = nc.dram_tensor("out_y", x.shape, F32, kind="ExternalOutput").ap()
    graph_attention(nc, *args, out)
    r = run_bass_kernel_spmd(nc, [{f"in_{n}": a for n, a in arrays.items()}], core_ids=[0])
    return r.results[0]["out_y"]
```

```python
from contextlib import ExitStack

import concourse.bass as bass
from concourse import mybir

F32 = mybir.dt.float32
F32R = mybir.dt.float32r
I32 = mybir.dt.int32
ALU = mybir.AluOpType
ACT = mybir.ActivationFunctionType

P = 128
EPS = 1e-5
MASKED = -(2.0 ** 126)


def graph_attention(nc, xT, x, adj, wqT, wkT, wvT, wo, bo, gamma, beta, out):
    B, L, D = x.shape
    C = D // P
    R = L // P
    assert L == D and C == R and B % 2 == 0
    SCALE = float(D) ** -0.5
    STEPS = R

    x_rows = x.rearrange("b (i p) d -> b p i d", p=P)
    adj_rows = adj.rearrange("b (i p) m -> b p i m", p=P)
    out_rows = out.rearrange("b (i p) d -> b p i d", p=P)

    with ExitStack() as ctx:
        def sb(name, shape, dt=F32):
            return ctx.enter_context(nc.sbuf_tensor(name, shape, dt))

        def sem(name):
            return ctx.enter_context(nc.semaphore(name))

        def split_pair(name):
            return sb(name + "_hi", [P, C, D], F32R), sb(name + "_lo", [P, C, D], F32R)

        m_qk = split_pair("m_qk")
        m_vo = split_pair("m_vo")
        x_t = [split_pair(f"x_t{k}") for k in range(2)]
        q_t = split_pair("q_t")
        v = [split_pair(f"v{k}") for k in range(2)]
        p_t = split_pair("p_t")
        x_t_raw = sb("x_t_raw", [P, C, L])
        adj_raw = sb("adj_raw", [P, R, L], I32)
        mask_add = sb("mask_add", [P, R, L])
        probs = sb("probs", [P, R, L])
        resid = [sb(f"resid{k}", [P, R, D]) for k in range(2)]
        y = [sb(f"y{k}", [P, R, D]) for k in range(2)]
        gamma_bc = sb("gamma_bc", [P, D])
        beta_bc = sb("beta_bc", [P, D])
        bo_bc = sb("bo_bc", [P, D])
        ident = sb("ident", [P, P])
        neg_max = sb("neg_max", [P, 2, R])
        row_sum = sb("row_sum", [P, 2, R])
        row_inv = sb("row_inv", [P, 2, R])
        stats = sb("stats", [P, 2, R, 6])
        mean_var = sb("mean_var", [P, 2, R, 2])
        var_eps = sb("var_eps", [P, 2, R])
        rstd = sb("rstd", [P, 2, R])
        neg_mean_rstd = sb("neg_mean_rstd", [P, 2, R])
        neg_mean = sb("neg_mean", [P, 2, R])
        minus_half = sb("minus_half", [P, R])
        minus_one = sb("minus_one", [P, R])
        eps = sb("eps", [P, R])
        wait_slot = sb("wait_slot", [P, 2, R, 2])
        banks = [ctx.enter_context(nc.psum_tensor(f"bank{k}", [P, 512], F32)) for k in range(8)]

        w_loaded = [sem(f"w_loaded{k}") for k in range(2 * C)]
        ln_loaded = sem("ln_loaded")
        xt_loaded = sem("xt_loaded")
        adj_loaded = sem("adj_loaded")
        x_loaded = sem("x_loaded")
        w_hi = sem("w_hi")
        w_lo = sem("w_lo")
        m_ps = sem("m_ps")
        m_hi = sem("m_hi")
        m_lo = sem("m_lo")
        xt_hi = sem("xt_hi")
        xt_lo = sem("xt_lo")
        q_ps = sem("q_ps")
        q_hi = sem("q_hi")
        q_lo = sem("q_lo")
        v_ps = sem("v_ps")
        v_hi = sem("v_hi")
        v_lo = sem("v_lo")
        s_ps = sem("s_ps")
        mask_ready = sem("mask_ready")
        masked = sem("masked")
        exp_done = sem("exp_done")
        pt_ps = sem("pt_ps")
        pt_hi = sem("pt_hi")
        pt_lo = sem("pt_lo")
        o_ps = sem("o_ps")
        inv_ready = sem("inv_ready")
        resid_ready = sem("resid_ready")
        y_ready = sem("y_ready")
        stats_ready = sem("stats_ready")
        moments_ready = sem("moments_ready")
        rstd_step = sem("rstd_step")
        last_var = sem("last_var")
        last_rstd = sem("last_rstd")
        last_scaled = sem("last_scaled")
        last_z = sem("last_z")
        last_out = sem("last_out")
        last_chunk_out = sem("last_chunk_out")
        last_stored = sem("last_stored")
        z_ready = sem("z_ready")
        scaled = sem("scaled")
        out_ready = sem("out_ready")
        stored = sem("stored")
        ident_zero = sem("ident_zero")
        ident_ready = sem("ident_ready")
        const_ready = sem("const_ready")

        w_raw = [resid[0], resid[1], y[0], y[1]]
        w_src = [wqT, wkT, wvT, wo]
        w_part = [v[0], v[1], p_t, q_t]

        early, late = range(C - 2), range(C - 2, C)

        def half_of(group):
            return banks[4 * (group % 2):4 * (group % 2) + 4]


        block = ctx.enter_context(nc.Block())

        @block.sync
        def _(sp):
            def load_xt(b):
                sp.dma_start(x_t_raw[:], xT[b]).then_inc(xt_loaded, 16)

            def load_adj(b):
                sp.dma_start(adj_raw[:], adj_rows[b]).then_inc(adj_loaded, 16)

            def load_x(b, par):
                sp.dma_start(resid[par][:], x_rows[b]).then_inc(x_loaded, 16)

            def store(b, par, first=False):
                if not first:
                    sp.wait_ge(stored, 16 * b)
                sp.wait_ge(out_ready, STEPS * b + STEPS)
                sp.dma_start(out_rows[b], y[par][:]).then_inc(stored, 16)

            def graph(b, par, ahead=2, behind=True, second=False):
                if ahead >= 1:
                    sp.wait_ge(mask_ready, b + 1)
                    load_adj(b + 1)
                    sp.wait_ge(resid_ready, STEPS * b + STEPS)
                    if behind:
                        sp.wait_ge(y_ready, STEPS * b)
                    load_x(b + 1, 1 - par)
                if ahead >= 2:
                    sp.wait_ge(xt_lo, STEPS * b + 2 * STEPS)
                    load_xt(b + 2)
                if behind:
                    store(b - 1, 1 - par, first=second)

            for k in range(2 * C):
                for w in (2 * (k // C), 2 * (k // C) + 1):
                    c = k % C
                    sp.dma_start(w_raw[w][:, c, :], w_src[w][P * c:P * c + P, :]).then_inc(w_loaded[k], 16)
            load_xt(0)
            for row, tile in ((gamma, gamma_bc), (beta, beta_bc), (bo, bo_bc)):
                sp.dma_start(tile[:], row.rearrange("(a d) -> a d", a=1).broadcast_to([P, D])).then_inc(ln_loaded, 16)
            load_adj(0)
            sp.wait_ge(xt_lo, STEPS)
            load_xt(1)
            sp.wait_ge(w_lo, 4 * C)
            load_x(0, 0)
            graph(0, 0, behind=False)
            graph(1, 1, second=True)
            with sp.Fori(2, B - 4, 2) as b:
                graph(b, 0)
                graph(b + 1, 1)
            graph(B - 4, 0)
            graph(B - 3, 1)
            graph(B - 2, 0, ahead=1)
            graph(B - 1, 1, ahead=0)
            for i in range(R):
                if i < R - 1:
                    sp.wait_ge(last_out, i + 1)
                else:
                    sp.wait_ge(last_chunk_out, 1)
                sp.dma_start(out_rows[B - 1][:, i, :], y[1][:, i, :]).then_inc(last_stored, 16)
            sp.wait_ge(stored, 16 * (B - 1))
            sp.wait_ge(last_stored, 16 * R)

        @block.tensor
        def _(pe):
            def product(bank, a, a_cols, b, signal):
                (a_hi, a_lo), (b_hi, b_lo) = a, b
                for c in range(C):
                    pe.matmul(bank[:], a_hi[:, c, a_cols], b_hi[:, c, :], start=(c == 0), stop=False)
                    pe.matmul(bank[:], a_hi[:, c, a_cols], b_lo[:, c, :], start=False, stop=False)
                    last = pe.matmul(bank[:], a_lo[:, c, a_cols], b_hi[:, c, :], start=False, stop=(c == C - 1))
                last.then_inc(signal, 1)

            def cols(k):
                return slice(P * k, P * k + P)

            def scores(b, par, half, first=False, last=False):
                pe.wait_ge(q_lo, STEPS * b + STEPS)
                if last:
                    pe.wait_ge(pt_lo, STEPS * b)
                elif not first:
                    pe.wait_ge(v_lo, STEPS * b + STEPS)
                for i in range(R):
                    product(half_of(half)[i], q_t, cols(i), x_t[par], s_ps)

            def queries(b, par, first=False, chunks=range(C)):
                pe.wait_ge(xt_lo, STEPS * b + STEPS)
                if first:
                    pe.wait_ge(v_lo, STEPS)
                else:
                    pe.wait_ge(y_ready, STEPS * b - STEPS)
                for e in chunks:
                    product(half_of(par)[e], m_qk, cols(e), x_t[par], q_ps)

            def transposes(b, half, last=False):
                if not last:
                    pe.wait_ge(exp_done, STEPS * b + STEPS)
                for i in range(R):
                    if last:
                        pe.wait_ge(exp_done, STEPS * b + i + 1)
                    for j in range(R):
                        done = pe.transpose(half_of(half)[i][:, cols(j)], probs[:, i, cols(j)], ident[:])
                    done.then_inc(pt_ps, 1)

            def values(b, par, half, free=None, chunks=range(R)):
                if free is not None:
                    pe.wait_ge(*free)
                for m in chunks:
                    if free is None and m % 2 == 0:
                        pe.wait_ge(q_lo, STEPS * b + m + 2)
                    product(half_of(half)[m], x_t[par], cols(m), m_vo, v_ps)

            def attend(b, par, half, freed=None):
                p_hi, p_lo = p_t
                v_hi_part, v_lo_part = v[par]
                if freed is None:
                    pe.wait_ge(pt_lo, STEPS * b + STEPS)
                for i in range(R):
                    if freed is not None:
                        pe.wait_ge(pt_lo, STEPS * b + i + 1)
                        pe.wait_ge(freed, STEPS * (B - 1) + i + 1)
                    bank = half_of(half)[i]
                    for j in range(R):
                        if freed is v_lo and i == 0:
                            pe.wait_ge(v_lo, STEPS * b + j + 1)
                        pe.matmul(bank[:], p_hi[:, i, cols(j)], v_hi_part[:, j, :], start=(j == 0), stop=False)
                        pe.matmul(bank[:], p_hi[:, i, cols(j)], v_lo_part[:, j, :], start=False, stop=False)
                        done = pe.matmul(bank[:], p_lo[:, i, cols(j)], v_hi_part[:, j, :], start=False, stop=(j == R - 1))
                    done.then_inc(o_ps, 1)

            for k in range(2):
                (a_hi, a_lo), (b_hi, b_lo) = w_part[2 * k], w_part[2 * k + 1]
                for c in range(C):
                    pe.wait_ge(w_lo, 2 * (C * k + c + 1))
                    for d in range(C):
                        bank = half_of(k)[d]
                        pe.matmul(bank[:], a_hi[:, c, cols(d)], b_hi[:, c, :], start=(c == 0), stop=False)
                        pe.matmul(bank[:], a_hi[:, c, cols(d)], b_lo[:, c, :], start=False, stop=False)
                        done = pe.matmul(bank[:], a_lo[:, c, cols(d)], b_hi[:, c, :], start=False, stop=(c == C - 1))
                        if c == C - 1:
                            done.then_inc(m_ps, 1)
            pe.wait_ge(m_lo, C)
            pe.wait_ge(xt_lo, STEPS)
            for e in range(C):
                product(half_of(0)[e], m_qk, cols(e), x_t[0], q_ps)
            values(0, 0, 1, free=(m_lo, 2 * C))
            pe.wait_ge(ident_ready, 1)

            def graph(b, par, first=False):
                scores(b, par, par, first=first)
                queries(b + 1, 1 - par, first=first)
                transposes(b, par)
                values(b + 1, 1 - par, 1 - par)
                attend(b, par, par)

            graph(0, 0, first=True)
            with pe.Fori(1, B - 3, 2) as b:
                graph(b, 1)
                graph(b + 1, 0)
            graph(B - 3, 1)
            scores(B - 2, 0, 0)
            queries(B - 1, 1, chunks=early)
            transposes(B - 2, 0)
            queries(B - 1, 1, chunks=late)
            attend(B - 2, 0, 1, freed=q_lo)
            scores(B - 1, 1, 0, last=True)
            values(B - 1, 1, 1, free=(y_ready, STEPS * (B - 1)), chunks=early)
            transposes(B - 1, 0, last=True)
            values(B - 1, 1, 1, free=(y_ready, STEPS * (B - 1)), chunks=late)
            attend(B - 1, 1, 1, freed=v_lo)

        @block.scalar
        def _(act):
            def high(dst, src, signal):
                act.activation(dst, src, ACT.Copy).then_inc(signal, 1)

            def split_xt(b, par):
                act.wait_ge(xt_loaded, 16 * b + 16)
                for c in range(C):
                    high(x_t[par][0][:, c, :], x_t_raw[:, c, :], xt_hi)

            def exponentials(b, par, half, first=False):
                if not first:
                    act.wait_ge(pt_ps, STEPS * b)
                for i in range(R):
                    act.wait_ge(masked, STEPS * b + i + 1)
                    act.activation(probs[:, i, :], half_of(half)[i][:], ACT.Exp, bias=neg_max[:, par, i:i + 1],
                                   scale=-1.0, accum_out=row_sum[:, par, i:i + 1]).then_inc(exp_done, 1)

            def normalise(b, par):
                act.wait_ge(rstd_step, 4 * b + 4)
                for i in range(R):
                    act.activation(y[par][:, i, :], y[par][:, i, :], ACT.Identity,
                                   bias=neg_mean_rstd[:, par, i:i + 1], scale=rstd[:, par, i:i + 1]).then_inc(z_ready, 1)

            def high_q(b, par, chunks=range(C)):
                for e in chunks:
                    act.wait_ge(q_ps, STEPS * b + e + 1)
                    high(q_t[0][:, e, :], half_of(par)[e][:], q_hi)

            def high_v(b, par, half, chunks=range(R)):
                for m in chunks:
                    act.wait_ge(v_ps, STEPS * b + m + 1)
                    high(v[par][0][:, m, :], half_of(half)[m][:], v_hi)

            def high_pt(b, half):
                for i in range(R):
                    act.wait_ge(pt_ps, STEPS * b + i + 1)
                    high(p_t[0][:, i, :], half_of(half)[i][:], pt_hi)

            for k in range(2 * C):
                act.wait_ge(w_loaded[k], 32)
                for w in (2 * (k // C), 2 * (k // C) + 1):
                    high(w_part[w][0][:, k % C, :], w_raw[w][:, k % C, :], w_hi)
            for d in range(C):
                act.wait_ge(m_ps, d + 1)
                high(m_qk[0][:, d, :], half_of(0)[d][:], m_hi)
            split_xt(0, 0)
            for d in range(C):
                act.wait_ge(m_ps, C + d + 1)
                high(m_vo[0][:, d, :], half_of(1)[d][:], m_hi)
            high_q(0, 0)
            high_v(0, 0, 1)
            split_xt(1, 1)

            def graph(b, par, ahead=2, behind=True):
                exponentials(b, par, par, first=not behind)
                if behind:
                    normalise(b - 1, 1 - par)
                if ahead < 2:
                    high_q(b + 1, 1 - par, early)
                    high_pt(b, par)
                    high_q(b + 1, 1 - par, late)
                    return
                high_q(b + 1, 1 - par)
                act.wait_ge(s_ps, STEPS * b + STEPS)
                split_xt(b + 2, par)
                high_pt(b, par)
                high_v(b + 1, 1 - par, 1 - par)

            graph(0, 0, behind=False)
            with act.Fori(1, B - 3, 2) as b:
                graph(b, 1)
                graph(b + 1, 0)
            graph(B - 3, 1)
            graph(B - 2, 0, ahead=1)
            exponentials(B - 1, 1, 0)
            normalise(B - 2, 0)
            high_v(B - 1, 1, 1, early)
            high_pt(B - 1, 0)
            high_v(B - 1, 1, 1, late)
            for i in range(R - 1):
                act.wait_ge(last_rstd, i + 1)
                act.wait_ge(last_scaled, i + 1)
                act.activation(y[1][:, i, :], y[1][:, i, :], ACT.Copy, scale=rstd[:, 1, i:i + 1]).then_inc(last_z, 1)

        @block.vector
        def _(dve):
            def low(dst, src, high_part, signal):
                dve.tensor_tensor(dst, src, high_part.bitcast(F32), ALU.subtract).then_inc(signal, 1)

            def split_xt(b, par):
                for c in range(C):
                    dve.wait_ge(xt_hi, STEPS * b + c + 1)
                    low(x_t[par][1][:, c, :], x_t_raw[:, c, :], x_t[par][0][:, c, :], xt_lo)

            def additive_mask(b):
                dve.wait_ge(adj_loaded, 16 * b + 16)
                dve.tensor_scalar(mask_add[:], adj_raw[:], 0.0, MASKED, ALU.is_equal, ALU.mult).then_inc(mask_ready, 1)

            def hold_wait(par, i, use):
                dve.memset(wait_slot[:, par, i, use:use + 1], 0.0)

            def mask_scores(b, par, i, half):
                if i == 0:
                    dve.wait_ge(mask_ready, b + 1)
                dve.wait_ge(s_ps, STEPS * b + i + 1)
                hold_wait(par, i, 0)
                bank = half_of(half)[i]
                dve.tensor_tensor_reduce(bank[:], bank[:], mask_add[:, i, :], -SCALE, 3.0e38, ALU.add, ALU.min,
                                         neg_max[:, par, i:i + 1]).then_inc(masked, 1)

            def moments(b, par, i):
                dve.wait_ge(y_ready, STEPS * b + i + 1)
                dve.bn_stats(stats[:, par, i, :], y[par][:, i, :]).then_inc(stats_ready, 1)
                dve.wait_ge(stats_ready, STEPS * b + i + 1)
                hold_wait(par, i, 1)
                dve.bn_aggr(mean_var[:, par, i, :], stats[:, par, i, :]).then_inc(moments_ready, 1)

            def low_q(b, par, chunks=range(C)):
                for e in chunks:
                    dve.wait_ge(q_hi, STEPS * b + e + 1)
                    low(q_t[1][:, e, :], half_of(par)[e][:], q_t[0][:, e, :], q_lo)

            def low_v(b, par, half, chunks=range(R)):
                for m in chunks:
                    dve.wait_ge(v_hi, STEPS * b + m + 1)
                    low(v[par][1][:, m, :], half_of(half)[m][:], v[par][0][:, m, :], v_lo)

            def low_pt(b, half):
                for i in range(R):
                    dve.wait_ge(pt_hi, STEPS * b + i + 1)
                    low(p_t[1][:, i, :], half_of(half)[i][:], p_t[0][:, i, :], pt_lo)

            def inverse_sums(b, par, reuse=True):
                dve.wait_ge(exp_done, STEPS * b + STEPS)
                dve.reciprocal(row_inv[:, par, :], row_sum[:, par, :]).then_inc(inv_ready, 1)
                dve.wait_ge(inv_ready, b + 1)
                dve.wait_ge(resid_ready, STEPS * b + STEPS)
                if reuse:
                    dve.wait_ge(stored, 16 * b - 16)

            def output(b, par, i, half):
                dve.wait_ge(o_ps, STEPS * b + i + 1)
                dve.scalar_tensor_tensor(y[par][:, i, :], half_of(half)[i][:], row_inv[:, par, i:i + 1],
                                         resid[par][:, i, :], ALU.mult, ALU.add).then_inc(y_ready, 1)

            for k in range(2 * C):
                for w in (2 * (k // C), 2 * (k // C) + 1):
                    dve.wait_ge(w_hi, 2 * k + w % 2 + 1)
                    low(w_part[w][1][:, k % C, :], w_raw[w][:, k % C, :], w_part[w][0][:, k % C, :], w_lo)
            for d in range(C):
                dve.wait_ge(m_hi, d + 1)
                low(m_qk[1][:, d, :], half_of(0)[d][:], m_qk[0][:, d, :], m_lo)
            split_xt(0, 0)
            for d in range(C):
                dve.wait_ge(m_hi, C + d + 1)
                low(m_vo[1][:, d, :], half_of(1)[d][:], m_vo[0][:, d, :], m_lo)
            additive_mask(0)
            low_q(0, 0)
            low_v(0, 0, 1)
            split_xt(1, 1)

            def graph(b, par, ahead=2, behind=True, reuse=True):
                for i in range(R):
                    mask_scores(b, par, i, par)
                    if behind:
                        moments(b - 1, 1 - par, i)
                if ahead >= 2:
                    low_q(b + 1, 1 - par)
                    additive_mask(b + 1)
                    split_xt(b + 2, par)
                    low_pt(b, par)
                    low_v(b + 1, 1 - par, 1 - par)
                else:
                    low_q(b + 1, 1 - par, early)
                    low_pt(b, par)
                    low_q(b + 1, 1 - par, late)
                    additive_mask(b + 1)
                inverse_sums(b, par, reuse)
                for i in range(R):
                    output(b, par, i, par if ahead >= 2 else 1 - par)

            graph(0, 0, behind=False, reuse=False)
            graph(1, 1, reuse=False)
            with dve.Fori(2, B - 2, 2) as b:
                graph(b, 0)
                graph(b + 1, 1)
            graph(B - 2, 0, ahead=1)
            for i in range(R):
                mask_scores(B - 1, 1, i, 0)
                moments(B - 2, 0, i)
            low_v(B - 1, 1, 1, early)
            low_pt(B - 1, 0)
            low_v(B - 1, 1, 1, late)
            inverse_sums(B - 1, 1)
            for i in range(R):
                chunk = y[1][:, i, :]
                output(B - 1, 1, i, 1)
                moments(B - 1, 1, i)
                dve.wait_ge(moments_ready, STEPS * (B - 1) + i + 1)
                dve.scalar_tensor_tensor(chunk, chunk, mean_var[:, 1, i, 0:1], gamma_bc[:],
                                         ALU.subtract, ALU.mult).then_inc(last_scaled, 1)
            dve.wait_ge(last_rstd, R)
            dve.wait_ge(last_scaled, R)
            dve.scalar_tensor_tensor(chunk, chunk, rstd[:, 1, R - 1:R], beta_bc[:],
                                     ALU.mult, ALU.add).then_inc(last_chunk_out, 1)

        @block.gpsimd
        def _(pool):
            pool.memset(minus_half[:], -0.5).then_inc(const_ready, 1)
            pool.memset(minus_one[:], -1.0).then_inc(const_ready, 1)
            pool.memset(eps[:], EPS).then_inc(const_ready, 1)
            pool.memset(ident[:], 0.0).then_inc(ident_zero, 1)
            pool.wait_ge(ident_zero, 1)
            pool.affine_select(out=ident[:], in_=ident[:], compare_op=ALU.not_equal, fill=1.0, base=0,
                               pattern=[[-1, P]], channel_multiplier=1).then_inc(ident_ready, 1)
            pool.wait_ge(const_ready, 3)
            pool.wait_ge(ln_loaded, 48)

            def residual(b, par):
                pool.wait_ge(x_loaded, 16 * b + 16)
                for i in range(R):
                    pool.tensor_tensor(resid[par][:, i, :], resid[par][:, i, :], bo_bc[:], ALU.add).then_inc(resid_ready, 1)

            def deviation(b, par):
                pool.wait_ge(moments_ready, STEPS * b + STEPS)
                pool.tensor_tensor(var_eps[:, par, :], mean_var[:, par, :, 1], eps[:], ALU.add).then_inc(rstd_step, 1)
                pool.wait_ge(rstd_step, 4 * b + 1)
                pool.tensor_tensor(rstd[:, par, :], var_eps[:, par, :], minus_half[:], ALU.pow).then_inc(rstd_step, 1)
                pool.tensor_tensor(neg_mean[:, par, :], mean_var[:, par, :, 0], minus_one[:], ALU.mult).then_inc(rstd_step, 1)
                pool.wait_ge(rstd_step, 4 * b + 3)
                pool.tensor_tensor(neg_mean_rstd[:, par, :], neg_mean[:, par, :], rstd[:, par, :], ALU.mult).then_inc(rstd_step, 1)

            def affine(b, par):
                for i in range(R):
                    pool.wait_ge(z_ready, STEPS * b + i + 1)
                    pool.tensor_tensor(y[par][:, i, :], y[par][:, i, :], gamma_bc[:], ALU.mult).then_inc(scaled, 1)
                for i in range(R):
                    pool.wait_ge(scaled, STEPS * b + i + 1)
                    pool.tensor_tensor(y[par][:, i, :], y[par][:, i, :], beta_bc[:], ALU.add).then_inc(out_ready, 1)

            residual(0, 0)
            with pool.Fori(0, B - 2, 2) as b:
                residual(b + 1, 1)
                deviation(b, 0)
                affine(b, 0)
                residual(b + 2, 0)
                deviation(b + 1, 1)
                affine(b + 1, 1)
            residual(B - 1, 1)
            deviation(B - 2, 0)
            affine(B - 2, 0)
            def last_deviation(i):
                pool.wait_ge(moments_ready, STEPS * (B - 1) + i + 1)
                pool.tensor_tensor(var_eps[:, 1, i:i + 1], mean_var[:, 1, i, 1:2], eps[:, 0:1], ALU.add).then_inc(last_var, 1)
                pool.wait_ge(last_var, i + 1)
                pool.tensor_tensor(rstd[:, 1, i:i + 1], var_eps[:, 1, i:i + 1], minus_half[:, 0:1], ALU.pow).then_inc(last_rstd, 1)

            def last_shift(i):
                pool.wait_ge(last_z, i + 1)
                pool.tensor_tensor(y[1][:, i, :], y[1][:, i, :], beta_bc[:], ALU.add).then_inc(last_out, 1)

            for i in range(R - 1):
                last_deviation(i)
                if i >= 1:
                    last_shift(i - 1)
            last_deviation(R - 1)
            last_shift(R - 2)


def kernel(x, adj, L0_gnn_Wq, L0_gnn_Wk, L0_gnn_Wv, L0_gnn_Wo, L0_gnn_bo, L0_gnn_gamma, L0_gnn_beta):
    import numpy as np
    import concourse.bacc as bacc
    from concourse.bass_utils import run_bass_kernel_spmd

    x = np.asarray(x)
    B, L, D = x.shape
    arrays = {
        "xT": np.ascontiguousarray(x.transpose(0, 2, 1).reshape(B, D // P, P, L).transpose(0, 2, 1, 3)),
        "x": np.ascontiguousarray(x),
        "adj": np.ascontiguousarray(np.asarray(adj)),
        "wqT": np.ascontiguousarray(np.asarray(L0_gnn_Wq).T),
        "wkT": np.ascontiguousarray(np.asarray(L0_gnn_Wk).T),
        "wvT": np.ascontiguousarray(np.asarray(L0_gnn_Wv).T),
        "wo": np.ascontiguousarray(np.asarray(L0_gnn_Wo)),
        "bo": np.ascontiguousarray(np.asarray(L0_gnn_bo)),
        "gamma": np.ascontiguousarray(np.asarray(L0_gnn_gamma)),
        "beta": np.ascontiguousarray(np.asarray(L0_gnn_beta)),
    }
    nc = bacc.Bacc("TRN2", target_bir_lowering=False, num_devices=1)
    args = [nc.dram_tensor(f"in_{n}", a.shape, mybir.dt.from_np(a.dtype), kind="ExternalInput").ap() for n, a in arrays.items()]
    out = nc.dram_tensor("out_y", x.shape, F32, kind="ExternalOutput").ap()
    graph_attention(nc, *args, out)
    r = run_bass_kernel_spmd(nc, [{f"in_{n}": a for n, a in arrays.items()}], core_ids=[0])
    return r.results[0]["out_y"]
```
